# Optimizing a Trainium2 kernel written in Bass

```python
import numpy as np
import jax
import jax.numpy as jnp

def _softmax(x, axis=-1):
    return jax.nn.softmax(x, axis=axis)

def _gelu(x):
    return jax.nn.gelu(x, approximate=True)

def _silu(x):
    return jax.nn.silu(x)

def _sigmoid(x):
    return jax.nn.sigmoid(x)

def _layernorm(x, axis=-1, eps=1e-05):
    m = jnp.mean(x, axis=axis, keepdims=True)
    v = jnp.var(x, axis=axis, keepdims=True)
    return (x - m) / jnp.sqrt(v + eps)

def _scatter_add(tgt, idx, src, axis=0):
    return tgt.at[idx].add(src)

def _segment_sum(src, seg, n):
    return jax.ops.segment_sum(src, seg, n)
kernel_name = 'mk_recurrent_d2_jaxref_r8_475f19'

def setup_inputs(seed: int=0):
    np.random.seed(seed)
    _w = jnp.asarray

    def _L0_attn_setup():
        import jax, jax.numpy as jnp
        import numpy as np
        EPS = 1e-05
        NUM_HEADS = 16
        FEATURE_DIM = 16
        CHUNK = 64

        def _phi(x):
            f = x.shape[-1]
            return (x[..., :, None] * x[..., None, :]).reshape(*x.shape[:-1], f * f)
        key = jax.random.key(seed)
        ks = jax.random.split(key, 5)
        b, l, d = (4, 256, 128)
        h, f = (NUM_HEADS, FEATURE_DIM)
        hd = d // h
        scale = 0.02
        return {'hidden_states': jax.random.normal(ks[0], (b, l, d), jnp.float32), 'Wq': jax.random.normal(ks[1], (d, h * f), jnp.float32) * scale, 'Wk': jax.random.normal(ks[2], (d, h * f), jnp.float32) * scale, 'Wv': jax.random.normal(ks[3], (d, h * hd), jnp.float32) * scale, 'Wo': jax.random.normal(ks[4], (h * hd, d), jnp.float32) * scale}
    _L0_attn_in = _L0_attn_setup()

    def _L0_ffn_setup():
        import jax, jax.numpy as jnp
        import numpy as np
        DIM = 128
        HIDDEN = 384
        SCALE = 1.0 / 127.0

        def _dequant(w_int, dtype):
            return w_int.astype(dtype) * jnp.asarray(SCALE, dtype)
        key = jax.random.key(seed)
        k_x, k_g, k_u, k_d = jax.random.split(key, 4)
        x = jax.random.normal(k_x, (4, 256, DIM), dtype=jnp.float32)
        w_gate = jax.random.randint(k_g, (HIDDEN, DIM), -127, 128, dtype=jnp.int32)
        w_up = jax.random.randint(k_u, (HIDDEN, DIM), -127, 128, dtype=jnp.int32)
        w_down = jax.random.randint(k_d, (DIM, HIDDEN), -127, 128, dtype=jnp.int32)
        return {'x': x, 'w_gate': w_gate, 'w_up': w_up, 'w_down': w_down}
    _L0_ffn_in = _L0_ffn_setup()

    def _L1_attn_setup():
        import jax, jax.numpy as jnp
        import numpy as np
        B, S, E = (4, 256, 128)
        H, KVH = (16, 4)
        D = E // H
        QL, KVL = (64, 32)
        ROPE_BASE = 10000.0

        def _rope(x):
            d = x.shape[-1]
            inv_freq = 1.0 / ROPE_BASE ** (jnp.arange(0, d, 2, dtype=jnp.float32) / d)
            t = jnp.arange(x.shape[1], dtype=jnp.float32)
            freqs = jnp.outer(t, inv_freq)
            cos = jnp.cos(freqs)[None, :, None, :].astype(x.dtype)
            sin = jnp.sin(freqs)[None, :, None, :].astype(x.dtype)
            x1, x2 = (x[..., ::2], x[..., 1::2])
            r1 = x1 * cos - x2 * sin
            r2 = x1 * sin + x2 * cos
            return jnp.stack([r1, r2], axis=-1).reshape(x.shape)
        key = jax.random.key(seed)
        ks = jax.random.split(key, 7)
        s = 0.02
        return {'x': jax.random.normal(ks[0], (B, S, E), dtype=jnp.float32), 'Wqa': jax.random.normal(ks[1], (E, QL), dtype=jnp.float32) * s, 'Wqb': jax.random.normal(ks[2], (QL, E), dtype=jnp.float32) * s, 'Wkva': jax.random.normal(ks[3], (E, KVL), dtype=jnp.float32) * s, 'Wkvb': jax.random.normal(ks[4], (KVL, KVH * D * 2), dtype=jnp.float32) * s, 'Wout': jax.random.normal(ks[5], (E, E), dtype=jnp.float32) * s, 'bout': jax.random.normal(ks[6], (E,), dtype=jnp.float32) * s}
    _L1_attn_in = _L1_attn_setup()

    def _L1_ffn_setup():
        import jax, jax.numpy as jnp
        import numpy as np
        B, T, D, F, E = (2, 128, 128, 512, 8)
        EPS = 1e-06
        key = jax.random.key(seed)
        k = jax.random.split(key, 5)
        scale = 0.02
        return {'x': jax.random.normal(k[0], (B, T, D), dtype=jnp.float32), 'rms_w': jnp.ones((D,), dtype=jnp.float32), 'gate_w': jax.random.normal(k[1], (E, D), dtype=jnp.float32) * scale, 'W1': jax.random.normal(k[2], (E, D, F), dtype=jnp.float32) * scale, 'b1': jnp.zeros((E, F), dtype=jnp.float32), 'W2': jax.random.normal(k[3], (E, F, D), dtype=jnp.float32) * scale, 'b2': jnp.zeros((E, D), dtype=jnp.float32)}
    _L1_ffn_in = _L1_ffn_setup()
    _d = {'L0_attn_hidden_states': _L0_attn_in['hidden_states'], 'L0_attn_Wq': _L0_attn_in['Wq'], 'L0_attn_Wk': _L0_attn_in['Wk'], 'L0_attn_Wv': _L0_attn_in['Wv'], 'L0_attn_Wo': _L0_attn_in['Wo'], 'L0_ffn_w_gate': _L0_ffn_in['w_gate'], 'L0_ffn_w_up': _L0_ffn_in['w_up'], 'L0_ffn_w_down': _L0_ffn_in['w_down'], 'L1_attn_Wqa': _L1_attn_in['Wqa'], 'L1_attn_Wqb': _L1_attn_in['Wqb'], 'L1_attn_Wkva': _L1_attn_in['Wkva'], 'L1_attn_Wkvb': _L1_attn_in['Wkvb'], 'L1_attn_Wout': _L1_attn_in['Wout'], 'L1_attn_bout': _L1_attn_in['bout'], 'L1_ffn_rms_w': _L1_ffn_in['rms_w'], 'L1_ffn_gate_w': _L1_ffn_in['gate_w'], 'L1_ffn_W1': _L1_ffn_in['W1'], 'L1_ffn_b1': _L1_ffn_in['b1'], 'L1_ffn_W2': _L1_ffn_in['W2'], 'L1_ffn_b2': _L1_ffn_in['b2']}
    _x0 = _d['L0_attn_hidden_states']
    _d['L0_attn_hidden_states'] = jax.random.normal(jax.random.fold_in(jax.random.key(seed), 1), (8, 512, 128), dtype=_x0.dtype)
    del _x0
    return _d

def reference(L0_attn_hidden_states, L0_attn_Wq, L0_attn_Wk, L0_attn_Wv, L0_attn_Wo, L0_ffn_w_gate, L0_ffn_w_up, L0_ffn_w_down, L1_attn_Wqa, L1_attn_Wqb, L1_attn_Wkva, L1_attn_Wkvb, L1_attn_Wout, L1_attn_bout, L1_ffn_rms_w, L1_ffn_gate_w, L1_ffn_W1, L1_ffn_b1, L1_ffn_W2, L1_ffn_b2):

    def _L0_attn_ref(hidden_states, Wq, Wk, Wv, Wo):
        import jax, jax.numpy as jnp
        import numpy as np
        EPS = 1e-05
        NUM_HEADS = 16
        FEATURE_DIM = 16
        CHUNK = 64

        def _phi(x):
            f = x.shape[-1]
            return (x[..., :, None] * x[..., None, :]).reshape(*x.shape[:-1], f * f)
        b, l, d = hidden_states.shape
        h, f = (NUM_HEADS, FEATURE_DIM)
        hd = d // h
        q = (hidden_states @ Wq).reshape(b, l, h, f).transpose(0, 2, 1, 3)
        k = (hidden_states @ Wk).reshape(b, l, h, f).transpose(0, 2, 1, 3)
        v = (hidden_states @ Wv).reshape(b, l, h, hd).transpose(0, 2, 1, 3)
        q = q * f ** (-0.5)
        n = l // CHUNK
        qc = q.reshape(b, h, n, CHUNK, f)
        kc = k.reshape(b, h, n, CHUNK, f)
        vc = v.reshape(b, h, n, CHUNK, hd)
        phi_q = _phi(qc)
        phi_k = _phi(kc)
        mask = jnp.tril(jnp.ones((CHUNK, CHUNK), dtype=q.dtype))

        def step(carry, inp):
            S, z = carry
            pq, pk, qi, ki, vi = inp
            inter_o = jnp.einsum('bhcf,bhfd->bhcd', pq, S)
            inter_z = jnp.einsum('bhcf,bhf->bhc', pq, z)
            A = jnp.einsum('bhcf,bhsf->bhcs', qi, ki) ** 2 * mask
            intra_o = jnp.einsum('bhcs,bhsd->bhcd', A, vi)
            intra_z = A.sum(-1)
            o = (inter_o + intra_o) / (inter_z + intra_z + EPS)[..., None]
            S = S + jnp.einsum('bhcf,bhcd->bhfd', pk, vi)
            z = z + pk.sum(2)
            return ((S, z), o)
        f2 = f * f
        S0 = jnp.zeros((b, h, f2, hd), q.dtype)
        z0 = jnp.zeros((b, h, f2), q.dtype)
        xs = (jnp.moveaxis(phi_q, 2, 0), jnp.moveaxis(phi_k, 2, 0), jnp.moveaxis(qc, 2, 0), jnp.moveaxis(kc, 2, 0), jnp.moveaxis(vc, 2, 0))
        _, o = jax.lax.scan(step, (S0, z0), xs)
        o = jnp.moveaxis(o, 0, 2).reshape(b, h, l, hd)
        o = o.transpose(0, 2, 1, 3).reshape(b, l, h * hd)
        return o @ Wo

    def _L0_ffn_ref(x, w_gate, w_up, w_down):
        import jax, jax.numpy as jnp
        import numpy as np
        DIM = 128
        HIDDEN = 384
        SCALE = 1.0 / 127.0

        def _dequant(w_int, dtype):
            return w_int.astype(dtype) * jnp.asarray(SCALE, dtype)
        wg = _dequant(w_gate, x.dtype)
        wu = _dequant(w_up, x.dtype)
        wd = _dequant(w_down, x.dtype)
        gate = jnp.einsum('bsd,hd->bsh', x, wg)
        up = jnp.einsum('bsd,hd->bsh', x, wu)
        h = jax.nn.silu(gate) * up
        return jnp.einsum('bsh,dh->bsd', h, wd)

    def _L1_attn_ref(x, Wqa, Wqb, Wkva, Wkvb, Wout, bout):
        import jax, jax.numpy as jnp
        import numpy as np
        B, S, E = (4, 256, 128)
        H, KVH = (16, 4)
        D = E // H
        QL, KVL = (64, 32)
        ROPE_BASE = 10000.0

        def _rope(x):
            d = x.shape[-1]
            inv_freq = 1.0 / ROPE_BASE ** (jnp.arange(0, d, 2, dtype=jnp.float32) / d)
            t = jnp.arange(x.shape[1], dtype=jnp.float32)
            freqs = jnp.outer(t, inv_freq)
            cos = jnp.cos(freqs)[None, :, None, :].astype(x.dtype)
            sin = jnp.sin(freqs)[None, :, None, :].astype(x.dtype)
            x1, x2 = (x[..., ::2], x[..., 1::2])
            r1 = x1 * cos - x2 * sin
            r2 = x1 * sin + x2 * cos
            return jnp.stack([r1, r2], axis=-1).reshape(x.shape)
        b, s, _ = x.shape
        scale = D ** (-0.5)
        q = (x @ Wqa @ Wqb).reshape(b, s, H, D)
        kv = (x @ Wkva @ Wkvb).reshape(b, s, KVH, D, 2)
        k, v = (kv[..., 0], kv[..., 1])
        q = _rope(q)
        k = _rope(k)
        g = H // KVH
        k = jnp.repeat(k, g, axis=2)
        v = jnp.repeat(v, g, axis=2)
        scores = jnp.einsum('bqhd,bkhd->bhqk', q, k) * scale
        causal = jnp.triu(jnp.ones((s, s), dtype=bool), k=1)
        scores = jnp.where(causal[None, None], -jnp.inf, scores)
        w = jax.nn.softmax(scores, axis=-1)
        out = jnp.einsum('bhqk,bkhd->bqhd', w, v).reshape(b, s, E)
        return out @ Wout + bout

    def _L1_ffn_ref(x, rms_w, gate_w, W1, b1, W2, b2):
        import jax, jax.numpy as jnp
        import numpy as np
        B, T, D, F, E = (2, 128, 128, 512, 8)
        EPS = 1e-06
        ms = jnp.mean(x * x, axis=-1, keepdims=True)
        xn = x * jax.lax.rsqrt(ms + EPS) * rms_w
        logits = jnp.einsum('btd,ed->bte', xn, gate_w)
        scores = jax.nn.softmax(logits, axis=-1)
        top1_idx = jnp.argmax(scores, axis=-1)
        top1_score = jnp.max(scores, axis=-1)
        out = jnp.zeros_like(xn)
        for e in range(E):
            h = jax.nn.silu(jnp.einsum('btd,df->btf', xn, W1[e]) + b1[e])
            ye = jnp.einsum('btf,fd->btd', h, W2[e]) + b2[e]
            out = jnp.where((top1_idx == e)[..., None], ye, out)
        return out * top1_score[..., None]
    x = L0_attn_hidden_states
    xn = _layernorm(x, axis=-1)
    s = _L0_attn_ref(xn, L0_attn_Wq, L0_attn_Wk, L0_attn_Wv, L0_attn_Wo)
    g = _silu(_L0_ffn_ref(xn, L0_ffn_w_gate, L0_ffn_w_up, L0_ffn_w_down))
    x = x + s * g
    xn = _layernorm(x, axis=-1)
    s = _L1_attn_ref(xn, L1_attn_Wqa, L1_attn_Wqb, L1_attn_Wkva, L1_attn_Wkvb, L1_attn_Wout, L1_attn_bout)
    g = _silu(_L1_ffn_ref(xn, L1_ffn_rms_w, L1_ffn_gate_w, L1_ffn_W1, L1_ffn_b1, L1_ffn_W2, L1_ffn_b2))
    x = x + s * g
    return x

_drawn_inputs = setup_inputs


def setup_inputs(seed=0):
    import zlib

    import numpy as np

    out = dict(_drawn_inputs(seed))
    spreads = {'L1_ffn_rms_w': (1.0, 0.6), 'L1_ffn_b1': (0.0, 0.8), 'L1_ffn_b2': (0.0, 0.8)}
    factors = {'L1_attn_Wqa': 8.0,
     'L1_attn_Wqb': 8.0,
     'L1_attn_Wkva': 8.0,
     'L1_attn_Wkvb': 8.0,
     'L1_attn_Wout': 8.0,
     'L1_attn_bout': 8.0,
     'L1_ffn_gate_w': 8.0,
     'L1_ffn_W1': 8.0,
     'L1_ffn_W2': 8.0}
    for name, (base, spread) in spreads.items():
        noise = np.random.default_rng([zlib.crc32(name.encode()), seed]).standard_normal(out[name].shape)
        drawn = base * np.exp(spread * noise) if base else spread * noise
        out[name] = jnp.asarray(drawn.astype(out[name].dtype))
    for name, factor in factors.items():
        out[name] = (out[name] * factor).astype(out[name].dtype)
    return out
```

```python
from contextlib import ExitStack

import numpy as np

import concourse.bass as bass
import concourse.mybir as mybir
from concourse.alu_op_type import AluOpType as ALU

ACT = mybir.ActivationFunctionType
AX = mybir.AxisListType
F32 = mybir.dt.float32
BF16 = mybir.dt.bfloat16
I32 = mybir.dt.int32

P = 128
B, T, D = 8, 512, 128
NB = T // P
H, FD, HD = 16, 16, 8
HID = 384
NC = HID // P
LN_EPS, ATT_EPS, RMS_EPS = 1e-5, 1e-5, 1e-6
Q_SCALE = FD ** -0.5
INT_SCALE = float(np.float32(1.0 / 127.0))

QUADS = H // 4
SLOTS = 10
RING = 4
GH = H // 2
PARTS = 6
Q_PART = (0, 0, 0, 1, 1, 2)
K_PART = (0, 1, 2, 0, 1, 0)
STACK_IN = 2 * PARTS * 16

MISC = ("xn2T", "xnT", "q0", "q1", "k0", "k1", "gate0", "up0", "outT0", "gate1", "up1", "outT1",
        "gate2", "up2", "outT2", "v", "f", "outT3", "oT", "s")


AHEAD = {name: -1 if name == "xn2T" else 0 if name[:2] in ("ou", "oT", "s") else 1 for name in MISC}


def misc_bank(name):
    return MISC.index(name) % 2


def bank_before(name, t):
    i, back = MISC.index(name), 0
    while True:
        i -= 2
        if i < 0:
            i, back = i + len(MISC), back + 1
        if t is None:
            return MISC[i], back
        if t - back < -1:
            return None
        if 0 <= t - back + AHEAD[MISC[i]] < B:
            return MISC[i], back


def slot_parts(slot):
    pair, s = divmod(slot, 5)
    h = 2 * pair
    return {0: [(h, 0, 0)], 1: [(h, 1, 0), (h, 3, 384)], 2: [(h + 1, 0, 0)], 3: [(h + 1, 1, 0), (h + 1, 3, 384)],
            4: [(h, 2, 0), (h + 1, 2, 256)]}[s]


def slot_of(h, j):
    for slot in range(SLOTS):
        for hh, jj, col in slot_parts(slot):
            if (hh, jj) == (h, j):
                return slot, col


class Signal:

    def __init__(self, sem, per_turn):
        self.sem, self.per = sem, per_turn

    def value(self, turn, k):
        return turn * self.per + k


class Made:

    def __init__(self, signal, k):
        self.sem, self.kind, self.k = signal.sem, signal, k

    def value(self, turn, one):
        return self.kind.value(turn, self.k + one)


def kind_of(name):
    return name.rstrip("0123456789") if name != "xn2T" else name


def made_signals(sem, block, names, kind):
    kinds = {}
    for name in names:
        kinds.setdefault(kind(name), []).append(name)
    return {name: Made(signal, k) for what, of in kinds.items()
            for signal in [Signal(sem(f"{what}_made_{block}"), len(of))] for k, name in enumerate(of)}


def wait(eng, signal, turn, k):
    eng.wait_ge(signal.sem, signal.value(turn, k))


def wait_apart(eng, signal, turn, k, passed):
    wait(eng, signal, turn, k)
    if not isinstance(turn, int):
        eng.sem_inc(passed, 1)


def program(nc, aps, out):
    with ExitStack() as ctx:
        sb = lambda name, shape, dt=F32: ctx.enter_context(nc.sbuf_tensor(name, shape, dt))
        kept = dict(
            sem=lambda name: ctx.enter_context(nc.semaphore(name)),
            x_all=sb("x_all", [P, B, NB, D]),
            xn2T_all=sb("xn2T_all", [P, B, T]),
            moments_all=sb("moments_all", [P, B, NB, 2]),
            scale2_all=sb("scale2_all", [P, B, NB]),
            ident=sb("ident", [P, P]))
        kept["passed"] = kept["sem"]("passed")
        first_block(nc, aps, kept)
        second_block(nc, aps, kept, out)


def first_block(nc, aps, kept):
    with ExitStack() as ctx:
        sb = lambda name, shape, dt=F32: ctx.enter_context(nc.sbuf_tensor(name, shape, dt))
        sem, passed = kept["sem"], kept["passed"]
        x_all, xn2T_all, moments_all, scale2_all, ident = (
            kept[k] for k in ("x_all", "xn2T_all", "moments_all", "scale2_all", "ident"))

        wqk_in = sb("wqk_in", [D, 2, 2 * P])
        wqk = sb("wqk", [D, 2, 2, P])
        wv = sb("wv", [D, P])
        wo = sb("wo", [P, D])
        w_int = sb("w_int", [P, 2 * NC + NC, P], I32)
        w_rows = sb("w_rows", [P, 2 * NC + NC, P])
        gate_up_T = sb("gate_up_T", [D, 2 * NC, P])
        down_T = sb("down_T", [P, NC, D])
        minus_half = sb("minus_half", [P, NB])
        v_ones = sb("v_ones", [P, NB, H, 32])
        q_stack = sb("q_stack", [PARTS * FD, H, T], BF16)
        k_stack = sb("k_stack", [PARTS * FD, H, T], BF16)
        parts = sb("parts", [P, 2, 3, 2, T], BF16)
        rest = sb("rest", [P, 2, 2, T])
        squares = sb("squares", [P, 2, SLOTS, T])
        stats = sb("stats", [P, 2, NB, 6])
        mean_var = sb("mean_var", [P, 2, NB, 2])
        var_eps = sb("var_eps", [P, 2, NB])
        rstd = sb("rstd", [P, NB])
        xn = sb("xn", [P, NB, D])
        xnT = sb("xnT", [D, T])
        gate_tanh = sb("gate_tanh", [P, T])
        gate_silu = sb("gate_silu", [P, T])
        hidT = sb("hidT", [P, NC, T])
        f_tanh = sb("f_tanh", [P, T])
        gate_all = sb("gate_all", [P, 2, NB, D])
        av_sb = sb("av_sb", [P, T])
        den = sb("den", [P, NB, 4])
        rden = sb("rden", [P, NB, 4])
        o_rows = sb("o_rows", [P, NB, D])
        oT = sb("oT", [P, T])
        sg = sb("sg", [P, NB, D])
        xn2 = sb("xn2", [P, NB, D])

        ring = ctx.enter_context(nc.psum_tensor("ring", [P, RING, T], F32))
        av = ctx.enter_context(nc.psum_tensor("av", [P, 2, T], F32))
        misc = ctx.enter_context(nc.psum_tensor("misc", [P, 2, T], F32))

        x_in = [sem(f"x_in{b}") for b in range(B)]
        w_in = sem("w_in")
        ident_done = sem("ident_done")
        const_done = sem("const_done")
        w_scaled = sem("w_scaled")
        w_turned = sem("w_turned")
        w_copied = sem("w_copied")
        stats_done = Signal(sem("stats_done"), NB)
        mean_done = Signal(sem("mean_done"), NB)
        rstd_step = Signal(sem("rstd_step"), 2)
        xn_done = Signal(sem("xn_done"), NB)
        made = made_signals(sem, "first", MISC, kind_of)
        xnT_done = Signal(sem("xnT_done"), 1)
        part1_done = Signal(sem("part1_done"), 4)
        rest_done = Signal(sem("rest_done"), 4)
        part2_done = Signal(sem("part2_done"), 4)
        part3_done = Signal(sem("part3_done"), 4)
        v_done = Signal(sem("v_done"), 1)
        gate_tanh_done = Signal(sem("gate_tanh_done"), NC)
        gate_silu_done = Signal(sem("gate_silu_done"), NC)
        hid_done = Signal(sem("hid_done"), NC)
        f_tanh_done = Signal(sem("f_tanh_done"), 1)
        gate_done = Signal(sem("gate_done"), 1)
        stack_in = [Signal(sem(f"stack_in{g}"), STACK_IN) for g in range(2)]
        scores_done = Signal(sem("scores_done"), QUADS * SLOTS)
        squares_done = Signal(sem("squares_done"), QUADS * SLOTS)
        masked = Signal(sem("masked"), QUADS * 2 * 3)
        av_done = Signal(sem("av_done"), QUADS)
        av_copied = Signal(sem("av_copied"), QUADS)
        den_done = Signal(sem("den_done"), QUADS)
        rden_done = Signal(sem("rden_done"), QUADS)
        o_done = Signal(sem("o_done"), QUADS)
        oT_done = Signal(sem("oT_done"), 1)
        sg_done = Signal(sem("sg_done"), 1)
        x1_done = Signal(sem("x1_done"), 1)
        stats2_done = Signal(sem("stats2_done"), NB)
        mean2_done = Signal(sem("mean2_done"), NB)
        rstd2_step = Signal(sem("rstd2_step"), 2)
        moments_kept = Signal(sem("moments_kept"), 1)
        xn2_done = Signal(sem("xn2_done"), NB)
        xn2T_done = Signal(sem("xn2T_done"), 1)

        read_by = {"xn2T": (xn2T_done, 1), "xnT": (xnT_done, 1), "v": (v_done, 1), "f": (gate_done, 1),
                   "oT": (oT_done, 1), "s": (sg_done, 1)}
        read_by |= {"qk"[i] + str(g): (rest_done, 2 * i + g + 1) for i in range(2) for g in range(2)}
        read_by |= {f"gate{u}": (gate_silu_done, u + 1) for u in range(NC)}
        read_by |= {f"up{u}": (hid_done, u + 1) for u in range(NC)}
        read_by |= {f"outT{c}": (o_done, c + 1) for c in range(QUADS)}

        wg, wu, wd = aps["L0_ffn_w_gate"], aps["L0_ffn_w_up"], aps["L0_ffn_w_down"]
        W_IN = 6 * 16

        block = ctx.enter_context(nc.Block())

        @block.sync
        def _(sp):
            for b in range(B):
                sp.dma_start(x_all[:, b], aps["L0_attn_hidden_states"][b].rearrange("(n p) d -> p n d", p=P))\
                    .then_inc(x_in[b], 16)
                if b == 0:
                    for i, name in enumerate(("L0_attn_Wq", "L0_attn_Wk")):
                        sp.dma_start(wqk_in[:, i], aps[name]).then_inc(w_in, 16)
                    sp.dma_start(wv[:], aps["L0_attn_Wv"]).then_inc(w_in, 16)
                    sp.dma_start(wo[:], aps["L0_attn_Wo"]).then_inc(w_in, 16)
                    sp.dma_start(w_int[:, 0:NC], wg.rearrange("(c p) d -> p c d", p=P)).then_inc(w_in, 16)
                    sp.dma_start(w_int[:, NC:2 * NC], wu.rearrange("(c p) d -> p c d", p=P)).then_inc(w_in, 16)
                    sp.dma_start(w_int[:, 2 * NC:], wd.rearrange("d (c p) -> d c p", p=P)).then_inc(w_in, 16)

            def stack(g):
                for i, (dst, order) in enumerate(((q_stack, Q_PART), (k_stack, K_PART))):
                    for r, part in enumerate(order):
                        sp.dma_start(dst[FD * r:FD * r + FD, GH * g:GH * g + GH, :], parts[:, i, part, g, :])\
                            .then_inc(stack_in[g].sem, 16)

            def turn(t, main):
                for g in range(2):
                    if main:
                        wait_apart(sp, scores_done, t, 2 * SLOTS * (g + 1), passed)
                    wait_apart(sp, part1_done, t + 1, 4, passed)
                    wait_apart(sp, part3_done, t + 1, 4, passed)
                    stack(g)

            turn(-1, False)
            with sp.Fori(0, B - 1) as t:
                turn(t, True)

        @block.tensor
        def _(pe):
            pe.wait_ge(ident_done, 2)
            for n in range(3 * NC):
                pe.wait_ge(w_scaled, 1)
                if n >= RING:
                    pe.wait_ge(w_copied, n - RING + 1)
                pe.transpose(ring[:, n % RING, 0:P], w_rows[:, n], ident[:]).then_inc(w_turned, 1)
            pe.wait_ge(w_copied, 3 * NC)
            pe.wait_ge(w_in, W_IN + 16)
            pe.wait_ge(const_done, 7)

            def take(name, t):
                before = bank_before(name, t if isinstance(t, int) else None)
                if before:
                    other, back = before
                    signal, k = read_by[other]
                    wait(pe, signal, t - back + AHEAD[other], k)
                return misc[:, misc_bank(name), :]

            def scores(t, c, slot):
                n = SLOTS * c + slot
                if slot == 0 and c % 2 == 0:
                    wait(pe, stack_in[c // 2], t, STACK_IN)
                if not (isinstance(t, int) and t == 0 and n < RING):
                    wait(pe, squares_done, t, n - RING + 1)
                pieces = slot_parts(slot)
                for k, (hh, j, col) in enumerate(pieces):
                    h, w = 4 * c + hh, T - P * j
                    last = pe.matmul(ring[:, n % RING, col:col + w], k_stack[:, h, P * j:P * j + P],
                                     q_stack[:, h, P * j:T], start=True, stop=True)
                last.then_inc(scores_done.sem, 1)

            def attend(t, c, j):
                if j == 0:
                    wait(pe, masked, t, 6 * (c + 1))
                    if not (isinstance(t, int) and t == 0 and c < 2):
                        wait(pe, av_copied, t, c - 1)
                    if c == 0:
                        wait(pe, v_done, t, 1)
                for hh in range(4):
                    slot, col = slot_of(hh, j)
                    last = pe.matmul(av[32 * hh:32 * hh + 32, c % 2, P * j:T], v_ones[:, j, 4 * c + hh, :],
                                     squares[:, c % 2, slot, col:col + T - P * j],
                                     start=(j == 0), stop=(j == NB - 1), skip_group_check=True)
                if j == NB - 1:
                    last.then_inc(av_done.sem, 1)

            def turn_blocks(name, t, source):
                bank = take(name, t)
                for i in range(NB):
                    last = pe.transpose(bank[:, P * i:P * i + P], source(i), ident[:])
                last.then_inc(made[name].sem, 1)

            def qk(t, i, g):
                bank = take("qk"[i] + str(g), t)
                if i == 0 and g == 0:
                    wait(pe, xnT_done, t + 1, 1)
                pe.matmul(bank, wqk[:, i, g], xnT[:], start=True, stop=True)\
                    .then_inc(made["qk"[i] + str(g)].sem, 1)

            def gate_up(t, u):
                for i, name in enumerate((f"gate{u}", f"up{u}")):
                    bank = take(name, t)
                    pe.matmul(bank, gate_up_T[:, NC * i + u], xnT[:], start=True, stop=True)\
                        .then_inc(made[name].sem, 1)

            def values(t):
                bank = take("v", t)
                for i in range(NB):
                    last = pe.matmul(bank[:, P * i:P * i + P], xnT[:, P * i:P * i + P], wv[:], start=(i == 0),
                                     stop=True, skip_group_check=True)
                last.then_inc(made["v"].sem, 1)

            def down(t):
                bank = take("f", t)
                wait(pe, hid_done, t + 1, NC)
                for i in range(NB):
                    for u in range(NC):
                        last = pe.matmul(bank[:, P * i:P * i + P], hidT[:, u, P * i:P * i + P], down_T[:, u],
                                         start=(i == 0 and u == 0), stop=(u == NC - 1), skip_group_check=True)
                last.then_inc(made["f"].sem, 1)

            def out_rows(t, c):
                wait(pe, av_copied, t, c + 1)
                turn_blocks(f"outT{c}", t, lambda i: av_sb[:, P * i:P * i + P])

            def project(t):
                wait(pe, o_done, t, QUADS)
                turn_blocks("oT", t, lambda i: o_rows[:, i])
                bank = take("s", t)
                wait(pe, oT_done, t, 1)
                for i in range(NB):
                    last = pe.matmul(bank[:, P * i:P * i + P], oT[:, P * i:P * i + P], wo[:], start=(i == 0),
                                     stop=True, skip_group_check=True)
                last.then_inc(made["s"].sem, 1)

            def post(t):
                wait(pe, xn2_done, t - 1, NB)
                turn_blocks("xn2T", t, lambda i: xn2[:, i])

            def xn_cols(t):
                wait(pe, xn_done, t + 1, NB)
                turn_blocks("xnT", t, lambda i: xn[:, i])

            def turn(t, main, prep, after):
                for c in range(QUADS):
                    for slot in range(SLOTS):
                        if main:
                            scores(t, c, slot)
                        if c == 0:
                            if slot == 1 and after:
                                post(t)
                            if slot == 3 and prep:
                                xn_cols(t)
                            if 5 <= slot <= 8 and prep:
                                qk(t, *divmod(slot - 5, 2))
                        else:
                            if slot == 0 and prep:
                                gate_up(t, c - 1)
                            if main and slot in (3, 5, 7, 8):
                                attend(t, c - 1, (3, 5, 7, 8).index(slot))
                            if slot == 9 and main:
                                out_rows(t, c - 1)
                if prep:
                    values(t)
                    down(t)
                if main:
                    for j in range(NB):
                        attend(t, QUADS - 1, j)
                    out_rows(t, QUADS - 1)
                    project(t)

            turn(-1, False, True, False)
            turn(0, True, True, False)
            with pe.Fori(1, B - 1) as t:
                turn(t, True, True, True)
            turn(B - 1, True, False, True)
            post(B)

        def misc_wait(eng, name, t):
            wait(eng, made[name], t + AHEAD[name], 1)
            return misc[:, misc_bank(name), :]

        @block.scalar
        def _(act):
            def square(t, c, slot):
                n = SLOTS * c + slot
                wait(act, scores_done, t, n + 1)
                if not (isinstance(t, int) and t == 0 and c < 2) and slot == 0:
                    wait(act, av_done, t, c - 1)
                nc.scalar.activation(squares[:, c % 2, slot], ring[:, n % RING], ACT.Square)\
                    .then_inc(squares_done.sem, 1)

            def copy_post(t):
                bank = misc_wait(act, "xn2T", t + 1)
                nc.scalar.copy(xn2T_all[:, t], bank).then_inc(xn2T_done.sem, 1)

            def copy_xn(t):
                bank = misc_wait(act, "xnT", t)
                nc.scalar.copy(xnT[:], bank).then_inc(xnT_done.sem, 1)

            def part1(t, i, g):
                bank = misc_wait(act, "qk"[i] + str(g), t)
                if i == 0 and g == 0 and not (isinstance(t, int) and t == -1):
                    for s in stack_in:
                        wait(act, s, t, STACK_IN)
                nc.scalar.copy(parts[:, i, 0, g], bank).then_inc(part1_done.sem, 1)

            def tanh_gate(t, u):
                bank = misc_wait(act, f"gate{u}", t)
                n = NC * 0 + u
                if not (isinstance(t, int) and t == -1 and u == 0):
                    wait(act, gate_silu_done, t + 1, n)
                nc.scalar.activation(gate_tanh[:], bank, ACT.Tanh, scale=0.5).then_inc(gate_tanh_done.sem, 1)

            def copy_v(t, main):
                bank = misc_wait(act, "v", t)
                if main:
                    wait(act, av_done, t, QUADS)
                nc.scalar.copy(v_ones[:, :, :, 0:HD], bank.rearrange("p (n h d) -> p n h d", n=NB, d=HD))\
                    .then_inc(v_done.sem, 1)

            def tanh_f(t):
                bank = misc_wait(act, "f", t)
                if not (isinstance(t, int) and t == -1):
                    wait(act, gate_done, t, 1)
                nc.scalar.activation(f_tanh[:], bank, ACT.Tanh, scale=0.5).then_inc(f_tanh_done.sem, 1)

            def copy_o(t):
                bank = misc_wait(act, "oT", t)
                nc.scalar.copy(oT[:], bank).then_inc(oT_done.sem, 1)

            def turn(t, main, prep, after):
                for c in range(QUADS):
                    for slot in range(SLOTS):
                        if main:
                            square(t, c, slot)
                        if c == 0:
                            if slot == 2 and after:
                                copy_post(t - 1)
                            if slot == 4 and prep:
                                copy_xn(t)
                            if 6 <= slot <= 9 and prep:
                                part1(t, *divmod(slot - 6, 2))
                        elif slot == 1 and prep:
                            tanh_gate(t, c - 1)
                if prep:
                    tanh_f(t)
                    copy_v(t, main)
                if main:
                    copy_o(t)

            turn(-1, False, True, False)
            turn(0, True, True, False)
            with act.Fori(1, B - 1) as t:
                turn(t, True, True, True)
            turn(B - 1, True, False, True)
            copy_post(B - 1)

        @block.vector
        def _(dve):
            nc.vector.memset(minus_half[:], -0.5).then_inc(const_done, 1)
            nc.vector.memset(v_ones[:], 0.0).then_inc(const_done, 1)
            dve.wait_ge(const_done, 2)
            nc.vector.memset(v_ones[:, :, :, HD:HD + 1], 1.0).then_inc(const_done, 1)
            dve.wait_ge(w_in, W_IN + 16)
            for i, factor in enumerate((Q_SCALE, 1.0)):
                for g in range(2):
                    nc.vector.tensor_scalar(wqk[:, i, g].rearrange("d (f h) -> d h f", h=GH),
                                            wqk_in[:, i, P * g:P * g + P].rearrange("d (h f) -> d h f", f=FD),
                                            factor, None, ALU.mult).then_inc(const_done, 1)
            nc.vector.tensor_scalar(w_rows[:], w_int[:], INT_SCALE, None, ALU.mult).then_inc(w_scaled, 1)
            for n in range(3 * NC):
                dve.wait_ge(w_turned, n + 1)
                src = ring[:, n % RING, 0:P]
                if n < 2 * NC:
                    nc.vector.tensor_copy(gate_up_T[:, n], src).then_inc(w_copied, 1)
                else:
                    nc.vector.tensor_scalar(down_T[:, n - 2 * NC], src, 0.5, None, ALU.mult).then_inc(w_copied, 1)

            def norm_stats(t):
                if isinstance(t, int):
                    dve.wait_ge(x_in[t], 16)
                for i in range(NB):
                    nc.vector.bn_stats(stats[:, 0, i], x_all[:, t, i]).then_inc(stats_done.sem, 1)
                for i in range(NB):
                    wait_apart(dve, stats_done, t, i + 1, passed)
                    nc.vector.bn_aggr(mean_var[:, 0, i], stats[:, 0, i]).then_inc(mean_done.sem, 1)

            def normalise(t):
                wait(dve, rstd_step, t, 2)
                if not (isinstance(t, int) and t == 0):
                    wait(dve, made["xnT"], t - 1, 1)
                for i in range(NB):
                    nc.vector.tensor_scalar(xn[:, i], x_all[:, t, i], mean_var[:, 0, i, 0:1], rstd[:, i:i + 1],
                                            ALU.subtract, ALU.mult).then_inc(xn_done.sem, 1)

            def rest_of(t, i, g):
                wait(dve, part1_done, t + 1, 2 * i + g + 1)
                if not (isinstance(t, int) and t == -1):
                    wait(dve, part3_done, t, 4)
                bank = misc[:, misc_bank("qk"[i] + str(g)), :]
                nc.vector.tensor_tensor(rest[:, i, g], bank, parts[:, i, 0, g], ALU.subtract)\
                    .then_inc(rest_done.sem, 1)

            def gated(t, u):
                bank = misc[:, misc_bank(f"gate{u}"), :]
                wait(dve, gate_tanh_done, t + 1, u + 1)
                nc.vector.scalar_tensor_tensor(out=gate_silu[:], in0=gate_tanh[:], scalar=1.0, in1=bank,
                                               op0=ALU.add, op1=ALU.mult).then_inc(gate_silu_done.sem, 1)
                bank = misc_wait(dve, f"up{u}", t)
                wait(dve, gate_silu_done, t + 1, u + 1)
                nc.vector.tensor_tensor(hidT[:, u], bank, gate_silu[:], ALU.mult).then_inc(hid_done.sem, 1)

            def gate_f(t, slot):
                bank = misc[:, misc_bank("f"), :]
                wait(dve, f_tanh_done, t + 1, 1)
                nc.vector.scalar_tensor_tensor(out=gate_all[:, slot], in0=f_tanh[:].rearrange("p (n d) -> p n d", n=NB),
                                               scalar=1.0, in1=bank.rearrange("p (n d) -> p n d", n=NB),
                                               op0=ALU.add, op1=ALU.mult).then_inc(gate_done.sem, 1)

            def copy_av(t, c):
                wait(dve, av_done, t, c + 1)
                if not (isinstance(t, int) and t == 0 and c == 0):
                    if c == 0:
                        wait(dve, made["outT3"], t - 1, 1)
                    else:
                        wait(dve, made[f"outT{c - 1}"], t, 1)
                nc.vector.tensor_copy(av_sb[:], av[:, c % 2]).then_inc(av_copied.sem, 1)

            def divide(t, c):
                bank = misc_wait(dve, f"outT{c}", t).rearrange("p (n h e) -> p n h e", n=NB, e=32)
                nc.vector.tensor_scalar(den[:], bank[:, :, :, HD], ATT_EPS, None, ALU.add).then_inc(den_done.sem, 1)
                wait(dve, den_done, t, c + 1)
                nc.vector.reciprocal(rden[:], den[:]).then_inc(rden_done.sem, 1)
                wait(dve, rden_done, t, c + 1)
                if c == 0 and not (isinstance(t, int) and t == 0):
                    wait(dve, made["oT"], t - 1, 1)
                for i in range(NB):
                    o = o_rows[:, i, 32 * c:32 * c + 32].rearrange("p (h d) -> p h d", d=HD)
                    ins = nc.vector.tensor_tensor(o, bank[:, i, :, 0:HD],
                                                  rden[:, i, :, None].to_broadcast([P, 4, HD]), ALU.mult)
                ins.then_inc(o_done.sem, 1)

            def finish(t, slot):
                bank = misc_wait(dve, "s", t).rearrange("p (n d) -> p n d", n=NB)
                nc.vector.scalar_tensor_tensor(out=sg[:], in0=bank, scalar=0.5, in1=gate_all[:, slot],
                                               op0=ALU.mult, op1=ALU.mult).then_inc(sg_done.sem, 1)
                wait(dve, sg_done, t, 1)
                nc.vector.tensor_tensor(x_all[:, t], sg[:], x_all[:, t], ALU.add).then_inc(x1_done.sem, 1)
                wait_apart(dve, x1_done, t, 1, passed)
                for i in range(NB):
                    nc.vector.bn_stats(stats[:, 1, i], x_all[:, t, i]).then_inc(stats2_done.sem, 1)
                for i in range(NB):
                    wait_apart(dve, stats2_done, t, i + 1, passed)
                    nc.vector.bn_aggr(mean_var[:, 1, i], stats[:, 1, i]).then_inc(mean2_done.sem, 1)
                wait(dve, rstd2_step, t, 2)
                nc.vector.tensor_copy(moments_all[:, t], mean_var[:, 1]).then_inc(moments_kept.sem, 1)
                if not (isinstance(t, int) and t == 0):
                    wait(dve, made["xn2T"], t - 1, 1)
                for i in range(NB):
                    nc.vector.tensor_scalar(xn2[:, i], x_all[:, t, i], mean_var[:, 1, i, 0:1],
                                            scale2_all[:, t, i:i + 1], ALU.subtract, ALU.mult)\
                        .then_inc(xn2_done.sem, 1)

            def turn(t, slot, main, prep):
                if prep:
                    norm_stats(t + 1)
                    normalise(t + 1)
                    for i in range(2):
                        for g in range(2):
                            rest_of(t, i, g)
                for c in range(1, QUADS):
                    if prep:
                        gated(t, c - 1)
                    if main:
                        copy_av(t, c - 1)
                        divide(t, c - 1)
                if prep:
                    gate_f(t, 1 - slot)
                if main:
                    copy_av(t, QUADS - 1)
                    divide(t, QUADS - 1)
                    finish(t, slot)

            turn(-1, 1, False, True)
            turn(0, 0, True, True)
            for b in range(2, B):
                dve.wait_ge(x_in[b], 16)
            with dve.Fori(0, (B - 2) // 2) as half:
                turn(half * 2 + 1, 1, True, True)
                turn(half * 2 + 2, 0, True, True)
            turn(B - 1, 1, True, False)

        @block.gpsimd
        def _(pool):
            nc.gpsimd.memset(ident[:], 0.0).then_inc(ident_done, 1)
            pool.wait_ge(ident_done, 1)
            nc.gpsimd.affine_select(out=ident[:], in_=ident[:], compare_op=ALU.not_equal, fill=1.0, base=0,
                                    pattern=[[-1, P]], channel_multiplier=1).then_inc(ident_done, 1)
            pool.wait_ge(const_done, 1)

            def inverse_std(t):
                wait_apart(pool, mean_done, t, NB, passed)
                nc.gpsimd.tensor_scalar(var_eps[:, 0], mean_var[:, 0, :, 1], LN_EPS, None, ALU.add)\
                    .then_inc(rstd_step.sem, 1)
                wait_apart(pool, rstd_step, t, 1, passed)
                if not (isinstance(t, int) and t == 0):
                    wait_apart(pool, xn_done, t - 1, NB, passed)
                nc.gpsimd.tensor_tensor(rstd[:], var_eps[:, 0], minus_half[:], ALU.pow).then_inc(rstd_step.sem, 1)

            def parts23(t, i, g):
                k = 2 * i + g + 1
                wait_apart(pool, rest_done, t + 1, k, passed)
                if i == 0 and g == 0 and not (isinstance(t, int) and t == -1):
                    for s in stack_in:
                        wait_apart(pool, s, t, STACK_IN, passed)
                nc.gpsimd.tensor_scalar(parts[:, i, 1, g], rest[:, i, g], 1.0, 1.0, ALU.mult, ALU.mult)\
                    .then_inc(part2_done.sem, 1)
                wait_apart(pool, part2_done, t + 1, k, passed)
                nc.gpsimd.tensor_tensor(parts[:, i, 2, g], rest[:, i, g], parts[:, i, 1, g], ALU.subtract)\
                    .then_inc(part3_done.sem, 1)

            def mask(t, c, pair):
                first = 5 * pair
                wait_apart(pool, squares_done, t, SLOTS * c + first + 5, passed)
                for view, n in ((squares[:, c % 2, first:first + 5, 0:P], 5),
                                (squares[:, c % 2, first + 1:first + 4:2, 384:512], 2),
                                (squares[:, c % 2, first + 4, 256:384], 0)):
                    pattern = [[0, n], [1, P]] if n else [[1, P]]
                    nc.gpsimd.affine_select(out=view, in_=view, compare_op=ALU.is_ge, fill=0.0, base=0,
                                            pattern=pattern, channel_multiplier=-1).then_inc(masked.sem, 1)

            def inverse_std2(t):
                wait_apart(pool, mean2_done, t, NB, passed)
                nc.gpsimd.tensor_scalar(var_eps[:, 1], mean_var[:, 1, :, 1], LN_EPS, None, ALU.add)\
                    .then_inc(rstd2_step.sem, 1)
                wait_apart(pool, rstd2_step, t, 1, passed)
                nc.gpsimd.tensor_tensor(scale2_all[:, t], var_eps[:, 1], minus_half[:], ALU.pow)\
                    .then_inc(rstd2_step.sem, 1)

            def turn(t, main, prep):
                if prep:
                    inverse_std(t + 1)
                for c in range(QUADS):
                    for pair in range(2):
                        if main:
                            mask(t, c, pair)
                        if c == 0 and prep:
                            parts23(t, pair, 0)
                            parts23(t, pair, 1)
                if main:
                    inverse_std2(t)

            turn(-1, False, True)
            turn(0, True, True)
            with pool.Fori(1, B - 1) as t:
                turn(t, True, True)
            turn(B - 1, True, False)


KH = 4
QL, KVL = 64, 32
ROPE_BASE = 10000.0
ROWS2 = PARTS * HD
STACK2_IN = 2 * PARTS * 16
EXP_SCALE = HD ** -0.5
E, FE = 8, 512
EC = FE // P
TILES = B * NB + E - 1
PER_TURN = 6
TURNS_OF_TILES = B - 1
assert PER_TURN * TURNS_OF_TILES >= TILES
TILES = PER_TURN * TURNS_OF_TILES
ROW = D + 1
NOBODY = 1 << 20
W_COLS = 2 * FE + EC + D
BIG = -1e30

UNITS = [(i, j) for i in range(NB) for j in range(i + 1)]
STEPS = len(UNITS) * KH
PV_RING = 3
MAX_BANKS = [(0, h) for h in range(0, H, 4)] + [(1, h) for h in range(0, H, 2)] + \
    [(i, h) for i in (2, 3) for h in range(H)]
HEADS_IN = (4, 2, 1, 1)
MAX_FROM = 14
TURN_AT = (1, 3, 5, 9)

MISC2 = ["a", "q", "q_swap", "k", "k_swap", "v"]


def max_banks(step):
    n, m = len(MAX_BANKS), STEPS - MAX_FROM
    if step < MAX_FROM:
        return range(0)
    return range((step - MAX_FROM) * n // m, (step - MAX_FROM + 1) * n // m)


def step_of_max(i):
    last = max(n for n, (ii, _) in enumerate(MAX_BANKS) if ii == i)
    return next(s for s in range(STEPS) if last in max_banks(s))


def events(step):
    out = [(name, 0) for name, s in (("a", 0), ("q", 2), ("q_swap", 3), ("k", 4), ("k_swap", 5), ("v", 6)) if s == step]
    for n in range(PER_TURN):
        out += [(kind, n) for kind, s in (("tx", 7 + 5 * n), ("th", 9 + 5 * n), ("ty", 11 + 5 * n)) if s == step]
    for i in range(NB - 1):
        if step == 4 * UNITS.index((i, i)) + 8:
            out.append(("o", i))
        if step == step_of_max(i) + 1:
            out.append(("m", i))
    return out


MISC2 = [f"{kind}{n}" for s in range(STEPS) for kind, n in events(s)] + ["m3", "o3", "oT0", "s0"]
assert len(MISC2) % 2 == 0 and len(set(MISC2)) == len(MISC2)


def stage2(name):
    return 0 if name in ("oT0", "s0") or name[0] in "ot" else 1


def exists2(name, t):
    if name[0] == "t":
        return 0 <= t < TURNS_OF_TILES
    return 0 <= t + stage2(name) < B


def bank_before2(name, t):
    i, back = MISC2.index(name), 0
    while True:
        i -= 2
        if i < 0:
            i, back = i + len(MISC2), back + 1
        if t is None:
            return MISC2[i], back
        if t - back < -1:
            return None
        if exists2(MISC2[i], t - back):
            return MISC2[i], back


def second_block(nc, aps, kept, out):
    sorted_rows = nc.dram_tensor("sorted_rows", (TILES * P, ROW), F32, kind="Internal").ap()
    expert_out = nc.dram_tensor("expert_out", (B * T, D), F32, kind="Internal").ap()
    with ExitStack() as ctx:
        sb = lambda name, shape, dt=F32: ctx.enter_context(nc.sbuf_tensor(name, shape, dt))
        sem, passed = kept["sem"], kept["passed"]
        x_all, xn2T_all, moments_all, scale2_all, ident = (
            kept[k] for k in ("x_all", "xn2T_all", "moments_all", "scale2_all", "ident"))

        wa = sb("wa", [D, QL + KVL])
        wqb_in = sb("wqb_in", [QL, P])
        wqb = sb("wqb", [QL, 2, P])
        wkvb_in = sb("wkvb_in", [QL + KVL, 2 * KH * HD])
        wkvb = sb("wkvb", [QL + KVL, 3, KH * HD])
        w_out = sb("w_out", [P, D])
        b_out = sb("b_out", [P, D])
        rope_q = sb("rope_q_sb", [P, 2, T])
        rope_k = sb("rope_k_sb", [KH * HD, 2, T])
        rms_w = sb("rms_w", [D, 1])
        gate_in = sb("gate_in", [E, D])
        gate_T = sb("gate_T", [D, E])
        b1_in = sb("b1_in", [E * EC, P])
        experts = sb("experts", [P, E, W_COLS])
        minus_half = sb("minus_half2", [P, B * NB])
        before = sb("before", [P, P])
        ones = sb("ones", [P, P])
        mask = sb("mask", [P, P], BF16)
        ident_b = sb("ident_b", [P, P], BF16)
        number = sb("number", [P, TILES])
        rms = sb("rms", [P, 3, B * NB])
        logits = sb("logits", [P, B * NB, E])
        top = sb("top", [P, B * NB])
        shifted = sb("shifted", [P, B * NB, E])
        expd = sb("expd", [P, B * NB, E])
        score = sb("score", [P, B * NB])
        esum = sb("esum", [P, B * NB])
        pick = sb("pick", [P, B * NB, E])
        first = sb("first", [P, B * NB])
        onehot = sb("onehot", [P, B * NB, E])
        HALF = B * NB // 2
        running = sb("running", [P, 2, HALF + B * NB, E])
        tiles_i = sb("tiles_i", [P, 2, E], I32)
        ends = sb("ends", [P, 3, 4 + E])
        place_f = sb("place_f", [P, B * NB, E])
        pos_f = sb("pos_f", [P, B * NB])
        pos = sb("pos", [P, B * NB], I32)
        over = sb("over", [P, TILES, E])
        tile_f = sb("tile_f", [P, TILES])
        tile_expert = sb("tile_expert", [P, TILES], I32)
        nobody = sb("nobody", [P, ROW])
        to_sort = sb("to_sort", [P, 4, ROW])
        aT = sb("aT", [QL + KVL, T])
        roped = sb("roped", [P, 3, T])
        roped_k = sb("roped_k", [KH * HD, 3, T])
        q_rest = sb("q_rest", [P, T])
        k_rest = sb("k_rest", [KH * HD, T])
        q_parts = sb("q_parts", [P, 3, T], BF16)
        k_parts = sb("k_parts", [KH * HD, 3, T], BF16)
        q_stack = sb("q_stack2", [ROWS2 + 2, 2, H, T], BF16)
        k_stack = sb("k_stack2", [64, 2, KH, T], BF16)
        v_ones = sb("v_ones2", [P, 2, NB, KH, 32])
        probs = sb("probs", [P, 2, KH, KH, P])
        maxima = sb("maxima", [P, NB, H])
        minus_max = sb("minus_max", [H, 2, NB, P], BF16)
        sums = sb("sums", [P, KH, P])
        rden = sb("rden2", [P, KH, KH])
        o_rows = sb("o_rows2", [P, NB, D])
        oT = sb("oT2", [P, T])
        tile_in = sb("tile_in", [P, 2, ROW])
        w_tile = sb("w_tile", [P, 2, W_COLS])
        tileT = sb("tileT", [D, P])
        pre = sb("pre", [P, EC, P])
        pre_tanh = sb("pre_tanh", [P, EC, P])
        hid = sb("hid", [P, EC, P])
        tile_out = sb("tile_out", [P, 2, D])
        y = roped[:, 0:2].rearrange("p s (n d) -> p s n d", n=NB)

        er = ctx.enter_context(nc.psum_tensor("er", [P, PV_RING, T], F32))
        mr = ctx.enter_context(nc.psum_tensor("mr", [P, 2, T], F32))
        pv = ctx.enter_context(nc.psum_tensor("pv", [P, T], F32))
        misc = ctx.enter_context(nc.psum_tensor("misc2", [P, 2, T], F32))

        w_in = sem("w2_in")
        experts_in = sem("experts_in")
        consts = sem("consts2")
        pool_consts = sem("pool_consts2")
        wqb_done = sem("wqb_done")
        turned = sem("turned")
        gate_ready = sem("gate_ready")
        b1_ready = sem("b1_ready")
        folded = sem("folded")
        logits_made = sem("logits_made")
        rms_step = sem("rms_step")
        route = sem("route")
        exp_route = sem("exp_route")
        counted = sem("counted")
        filled = sem("filled")
        to_sort_done = sem("to_sort_done")
        sorted_in = [sem(f"sorted_in{i}") for i in range(4)]

        made = made_signals(sem, "second", MISC2, kind_of)
        aT_done = Signal(sem("aT_done"), 1)
        rope_mult = Signal(sem("rope_mult"), 4)
        rope_add = Signal(sem("rope_add"), 2)
        part1_done = Signal(sem("part1_done2"), 2)
        rest_done = Signal(sem("rest_done2"), 2)
        part2_done = Signal(sem("part2_done2"), 2)
        part3_done = Signal(sem("part3_done2"), 2)
        stack_in = Signal(sem("stack_in2"), STACK2_IN)
        v_done = Signal(sem("v_done2"), 1)
        max_made = Signal(sem("max_made"), len(MAX_BANKS))
        max_done = Signal(sem("max_done"), len(MAX_BANKS))
        minus1_done = Signal(sem("minus1_done"), NB)
        minus2_done = Signal(sem("minus2_done"), NB)
        max_in = [Signal(sem(f"max_in{i}"), 32) for i in range(NB)]
        scores_done = Signal(sem("scores_done2"), STEPS)
        exp_done = Signal(sem("exp_done"), STEPS)
        masked = Signal(sem("masked2"), NB * KH)
        pv_unit = Signal(sem("pv_unit"), len(UNITS))
        sums_done = Signal(sem("sums_done"), NB)
        rden_done = Signal(sem("rden_done2"), NB)
        o_done = Signal(sem("o_done2"), NB)
        oT_done = Signal(sem("oT_done2"), 1)
        s_done = Signal(sem("s_done"), 1)
        tile_in_done = [Signal(sem(f"tile_in_done{i}"), 32 * PER_TURN // 2) for i in range(2)]
        tileT_done = Signal(sem("tileT_done"), PER_TURN)
        pre_done = Signal(sem("pre_done"), PER_TURN)
        pre_tanh_done = Signal(sem("pre_tanh_done"), PER_TURN)
        hid_done = Signal(sem("hid_done2"), PER_TURN)
        tile_done = Signal(sem("tile_done"), PER_TURN)
        tile_out_done = [Signal(sem(f"tile_out_done{i}"), 16 * PER_TURN // 2) for i in range(2)]

        y_in = [Signal(sem(f"y_in{i}"), 16) for i in range(2)]
        y_scaled = Signal(sem("y_scaled"), 1)
        y_tanh_done = Signal(sem("y_tanh_done"), 1)
        y_silu_done = Signal(sem("y_silu_done"), 1)
        gated_done = Signal(sem("gated_done"), 1)
        result_done = Signal(sem("result_done"), 1)
        out_written = sem("out_written")

        read_by = {"a0": (aT_done, 1), "v0": (v_done, 1), "oT0": (oT_done, 1), "s0": (s_done, 1)}
        read_by |= {name: (rope_mult, k + 1) for k, name in enumerate(("q0", "q_swap0", "k0", "k_swap0"))}
        read_by |= {f"m{i}": (minus2_done, i + 1) for i in range(NB)}
        read_by |= {f"o{i}": (o_done, i + 1) for i in range(NB)}
        for n in range(PER_TURN):
            read_by |= {f"tx{n}": (tileT_done, n + 1), f"th{n}": (pre_done, n + 1), f"ty{n}": (tile_done, n + 1)}

        def bank_of(name):
            return misc[:, MISC2.index(name) % 2, :]

        def misc_wait(eng, name, t):
            wait(eng, made[name], t + stage2(name), 1)
            return bank_of(name)

        def fixed(t):
            return isinstance(t, int)

        N_W = 9
        block = ctx.enter_context(nc.Block())

        @block.sync
        def _(sp):
            load = lambda dst, src: sp.dma_start(dst, src).then_inc(w_in, 16)
            load(wa[:, 0:QL], aps["L1_attn_Wqa"])
            load(wa[:, QL:], aps["L1_attn_Wkva"])
            load(wqb_in[:], aps["L1_attn_Wqb"])
            load(wkvb_in[QL:, :], aps["L1_attn_Wkvb"])
            load(gate_in[:], aps["L1_ffn_gate_w"])
            load(rms_w[:], aps["L1_ffn_rms_w"].rearrange("(d a) -> d a", a=1))
            load(b1_in[:], aps["L1_ffn_b1"].rearrange("e (c p) -> (e c) p", p=P))
            load(rope_q[:], aps["rope_q"])
            load(rope_k[:], aps["rope_k"])
            sp.wait_ge(consts, N_CONSTS)
            sp.dma_start(sorted_rows.rearrange("(n p) c -> p n c", p=P),
                         nobody[:, None, :].to_broadcast([P, TILES, ROW])).then_inc(filled, 16)
            load2 = lambda dst, src: sp.dma_start(dst, src).then_inc(experts_in, 16)
            load2(experts[:, :, 0:FE], aps["L1_ffn_W1"].rearrange("e d f -> d e f"))
            load2(w_out[:], aps["L1_attn_Wout"])
            load2(b_out[:], aps["L1_attn_bout"].rearrange("(a d) -> a d", a=1).to_broadcast([P, D]))
            load2(experts[:, :, 2 * FE + EC:], aps["L1_ffn_b2"].rearrange("(a e) d -> a e d", a=1).to_broadcast([P, E, D]))
            for e in range(E):
                load2(experts[:, e, FE:2 * FE].rearrange("p (c d) -> p c d", c=EC),
                      aps["L1_ffn_W2"][e].rearrange("(c p) d -> p c d", p=P))

            def stack(t, par):
                wait_apart(sp, part1_done, t + 1, 2, passed)
                wait_apart(sp, part3_done, t + 1, 2, passed)
                if not (fixed(t) and t < 1):
                    wait_apart(sp, scores_done, t - 1, STEPS, passed)
                for dst, src, order in ((q_stack, q_parts, Q_PART), (k_stack, k_parts, K_PART)):
                    for r, part in enumerate(order):
                        sp.dma_start(dst[HD * r:HD * r + HD, 1 - par], src[:, part]).then_inc(stack_in.sem, 16)

            def max_rows(t, par, i):
                wait_apart(sp, minus1_done, t + 1, i + 1, passed)
                wait_apart(sp, minus2_done, t + 1, i + 1, passed)
                for part in range(2):
                    sp.dma_start(q_stack[ROWS2 + part:ROWS2 + part + 1, 1 - par, :, P * i:P * i + P],
                                 minus_max[:, part, i]).then_inc(max_in[i].sem, 16)

            def fetch_tile(t, n):
                if not (fixed(t) and t == 0 and n < 2):
                    wait_apart(sp, tile_done, t, n - 1, passed)
                    wait_apart(sp, tile_out_done[n % 2], t, 16 * (n // 2), passed)
                expert = sp.value_load(tile_expert[0:1, bass.ds(t * PER_TURN + n, 1)], min_val=0, max_val=E - 1)
                sp.dma_start(w_tile[:, n % 2], experts[:, expert, :]).then_inc(tile_in_done[n % 2].sem, 16)
                sp.dma_start(tile_in[:, n % 2], sorted_rows.rearrange("(n p) c -> n p c", p=P)[t * PER_TURN + n])\
                    .then_inc(tile_in_done[n % 2].sem, 16)

            def turn(t, par, main, prep, tiles):
                if tiles:
                    fetch_tile(t, 0)
                    fetch_tile(t, 1)
                if prep:
                    stack(t, par)
                for step in range(STEPS):
                    for kind, n in events(step):
                        if kind == "m" and prep:
                            max_rows(t, par, n)
                        if kind == "ty" and tiles and n + 2 < PER_TURN:
                            fetch_tile(t, n + 2)
                if prep:
                    max_rows(t, par, NB - 1)

            turn(-1, 1, False, True, False)
            sp.wait_ge(route, ROUTE_EXPERTS)
            sp.wait_ge(folded, 2)
            sp.wait_ge(b1_ready, 1)
            sp.wait_ge(experts_in, 12 * 16)
            for i in range(4):
                sp.wait_ge(sorted_in[i], 16 * B * NB // 4)
            turn(0, 0, True, True, True)
            with sp.Fori(0, (B - 2) // 2) as half:
                turn(half * 2 + 1, 1, True, True, True)
                turn(half * 2 + 2, 0, True, True, True)

            for i in range(2):
                wait_apart(sp, tile_out_done[i], TURNS_OF_TILES, 0, passed)

            def load_y(b, pair, par):
                if not (fixed(b) and b < 2):
                    wait_apart(sp, y_silu_done, b - 2, 1, passed)
                sp.dma_start(y[:, par], expert_out.rearrange("(b n p) d -> b p n d", n=NB, p=P)[b])\
                    .then_inc(y_in[par].sem, 16)

            def store(b):
                wait_apart(sp, result_done, b, 1, passed)
                sp.dma_start(out.rearrange("b (n p) d -> b p n d", p=P)[b], x_all[:, b]).then_inc(out_written, 16)

            load_y(0, 0, 0)
            load_y(1, 0, 1)
            with sp.Fori(1, B // 2) as pair:
                for par in range(2):
                    load_y(pair * 2 + par, pair, par)
                    store(pair * 2 + par - 2)
            store(B - 2)
            store(B - 1)
            sp.wait_ge(out_written, 16 * B)

        @block.tensor
        def _(pe):
            pe.wait_ge(w_in, 16 * N_W)
            pe.transpose(mr[:, 0, 0:E], gate_in[:], ident[0:E, 0:E]).then_inc(turned, 1)
            pe.transpose(mr[:, 1, 0:E * EC], b1_in[:], ident[0:E * EC, 0:E * EC]).then_inc(turned, 1)
            pe.wait_ge(gate_ready, 1)
            for n in range(B * NB):
                last = pe.matmul(er[:, 0, E * n:E * n + E], xn2T_all[:, n // NB, P * (n % NB):P * (n % NB) + P],
                                 gate_T[:], start=(n == 0), stop=True, skip_group_check=True)
            last.then_inc(logits_made, 1)

            def pe_wait_apart(eng, signal, turn, k):
                wait_apart(eng, signal, turn, k, passed)

            def take(name, t):
                how = pe_wait_apart if kind_of(name) in ("k", "k_swap") else wait
                found = bank_before2(name, t if fixed(t) else None)
                if found:
                    other, back = found
                    signal, k = read_by[other]
                    how(pe, signal, t - back + stage2(other), k)
                return bank_of(name)

            def done(ins, name):
                ins.then_inc(made[name].sem, 1)

            def first_projection(t):
                bank = take("a0", t)
                done(pe.matmul(bank[0:QL + KVL], wa[:], xn2T_all[:, t + 1, :], start=True, stop=True), "a0")

            def project_q(t, swap):
                name = ("q0", "q_swap0")[swap]
                bank = take(name, t)
                if not swap:
                    wait(pe, aT_done, t + 1, 1)
                done(pe.matmul(bank, wqb[:, swap], aT[0:QL], start=True, stop=True), name)

            def project_k(t, swap):
                name = ("k0", "k_swap0")[swap]
                bank = take(name, t)
                done(pe.matmul(bank[0:KH * HD], wkvb[QL:, swap], aT[QL:], start=True, stop=True), name)

            def project_v(t):
                bank = take("v0", t)
                for i in range(NB):
                    last = pe.matmul(bank[:, 32 * i:32 * i + 32], aT[QL:, P * i:P * i + P], wkvb[QL:, 2],
                                     start=(i == 0), stop=True, skip_group_check=True)
                done(last, "v0")

            def max_scores(t, par, n):
                i, h0 = MAX_BANKS[n]
                heads, keys = HEADS_IN[i], P * (i + 1)
                if n == 0:
                    wait(pe, stack_in, t + 1, STACK2_IN)
                if not (fixed(t) and t == -1 and n < 2):
                    wait(pe, max_done, t + 1, n - 1)
                bank = mr[:, n % 2, 0:heads * keys].rearrange("p (h k) -> p h k", h=heads)
                pe.matmul(bank[:, :, keys - P:keys], ident_b[:], mask[:, None, :].to_broadcast([P, heads, P]),
                          start=True, stop=False, skip_group_check=True)
                for h in range(heads):
                    last = pe.matmul(bank[:, h, :], q_stack[0:ROWS2, 1 - par, h0 + h, P * i:P * i + P],
                                     k_stack[0:ROWS2, 1 - par, (h0 + h) // KH, 0:keys],
                                     start=False, stop=True, skip_group_check=True)
                last.then_inc(max_made.sem, 1)

            def turn_maxima(t, i):
                bank = take(f"m{i}", t)
                last = max(n for n, (ii, _) in enumerate(MAX_BANKS) if ii == i)
                wait(pe, max_done, t + 1, last + 1)
                done(pe.transpose(bank[0:H, 0:P], maxima[:, i], ident[:]), f"m{i}")

            def exp_scores(t, par, n):
                (i, j), g = UNITS[n // KH], n % KH
                if g == 0 and j == 0:
                    wait(pe, max_in[i], t, 32)
                if n >= PV_RING:
                    wait(pe, exp_done, t, n - PV_RING + 1)
                elif not (fixed(t) and t == 0):
                    wait(pe, exp_done, t - 1, max(k for k in range(STEPS) if k % PV_RING == n) + 1)
                pe.matmul(er[:, n % PV_RING].rearrange("p (h q) -> p h q", h=KH), k_stack[0:ROWS2 + 2, par, g, P * j:P * j + P],
                          q_stack[:, par, KH * g:KH * g + KH, P * i:P * i + P], start=True, stop=True)\
                    .then_inc(scores_done.sem, 1)

            def weigh(t, par, u):
                i, j = UNITS[u]
                if i == j:
                    wait(pe, masked, t, KH * (i + 1))
                else:
                    wait(pe, exp_done, t, KH * (u + 1))
                if u == 0:
                    wait(pe, v_done, t, 1)
                if j == 0 and not (fixed(t) and t == 0 and i == 0):
                    wait(pe, sums_done, t, i)
                for g in range(KH):
                    last = pe.matmul(pv[32 * g:32 * g + 32, :], v_ones[:, par, j, g, :],
                                     probs[:, u % 2, g].rearrange("p h q -> p (h q)"), start=(j == 0), stop=(j == i),
                                     skip_group_check=True)
                last.then_inc(pv_unit.sem, 1)

            def turn_sums(t, i):
                bank = take(f"o{i}", t)
                wait(pe, sums_done, t, i + 1)
                for h in range(KH):
                    last = pe.transpose(bank[:, P * h:P * h + P], sums[:, h], ident[:])
                done(last, f"o{i}")

            def project_out(t):
                bank = take("oT0", t)
                wait(pe, o_done, t, NB)
                for i in range(NB):
                    last = pe.transpose(bank[:, P * i:P * i + P], o_rows[:, i], ident[:])
                done(last, "oT0")
                bank = take("s0", t)
                wait(pe, oT_done, t, 1)
                for i in range(NB):
                    last = pe.matmul(bank[:, P * i:P * i + P], oT[:, P * i:P * i + P], w_out[:], start=(i == 0),
                                     stop=True, skip_group_check=True)
                done(last, "s0")

            def tile_turn(t, n):
                bank = take(f"tx{n}", t)
                wait(pe, tile_in_done[n % 2], t, 32 * (n // 2 + 1))
                done(pe.transpose(bank[:, 0:P], tile_in[:, n % 2, 0:D], ident[:]), f"tx{n}")

            def tile_hidden(t, n):
                bank = take(f"th{n}", t)
                wait(pe, tileT_done, t, n + 1)
                for c in range(EC):
                    last = pe.matmul(bank[:, P * c:P * c + P], w_tile[:, n % 2, P * c:P * c + P], tileT[:],
                                     start=(c == 0), stop=True, skip_group_check=True)
                done(last, f"th{n}")

            def tile_back(t, n):
                bank = take(f"ty{n}", t)
                wait(pe, hid_done, t, n + 1)
                for c in range(EC):
                    last = pe.matmul(bank[:, 0:D], hid[:, c], w_tile[:, n % 2, FE + D * c:FE + D * c + D],
                                     start=(c == 0), stop=(c == EC - 1))
                done(last, f"ty{n}")

            def turn(t, par, main, prep, tiles):
                for step in range(STEPS):
                    if main:
                        exp_scores(t, par, step)
                    if prep:
                        for n in max_banks(step):
                            max_scores(t, par, n)
                    if main and step % 4 == 2 and step > 4:
                        weigh(t, par, step // 4 - 1)
                    for kind, n in events(step):
                        if kind in "aqkv" or "swap" in kind:
                            if prep:
                                {"a": lambda: first_projection(t), "q": lambda: project_q(t, 0),
                                 "q_swap": lambda: project_q(t, 1), "k": lambda: project_k(t, 0),
                                 "k_swap": lambda: project_k(t, 1), "v": lambda: project_v(t)}[kind]()
                        elif kind == "m" and prep:
                            turn_maxima(t, n)
                        elif kind == "o" and main:
                            turn_sums(t, n)
                        elif kind == "tx" and tiles:
                            tile_turn(t, n)
                        elif kind == "th" and tiles:
                            tile_hidden(t, n)
                        elif kind == "ty" and tiles:
                            tile_back(t, n)
                if main:
                    weigh(t, par, len(UNITS) - 1)
                if prep:
                    turn_maxima(t, NB - 1)
                if main:
                    turn_sums(t, NB - 1)
                    project_out(t)

            pe.wait_ge(wqb_done, 6)
            pe.wait_ge(b1_ready, 1)
            turn(-1, 1, False, True, False)
            pe.wait_ge(route, ROUTE_ONEHOT)
            pe.wait_ge(pool_consts, 6)
            flat = onehot[:].rearrange("p n e -> p (n e)")
            pe.matmul(er[:, 1, 0:B * NB * E], before[:], flat, start=True, stop=True)
            pe.matmul(er[:, 2, 0:B * NB * E], ones[:], flat, start=True, stop=True).then_inc(counted, 1)
            pe.wait_ge(route, ROUTE_PLACE)
            turn(0, 0, True, True, True)
            with pe.Fori(0, (B - 2) // 2) as half:
                turn(half * 2 + 1, 1, True, True, True)
                turn(half * 2 + 2, 0, True, True, True)
            turn(B - 1, 1, True, False, False)

        @block.scalar
        def _(act):
            def copy_a(t):
                bank = misc_wait(act, "a0", t)
                if not (fixed(t) and t == -1):
                    wait(act, made["v0"], t, 1)
                nc.scalar.copy(aT[:], bank[0:QL + KVL]).then_inc(aT_done.sem, 1)

            def part1(t, k):
                wait(act, rope_add, t + 1, k + 1)
                if not (fixed(t) and t == -1):
                    wait(act, stack_in, t, STACK2_IN)
                dst, src = ((q_parts, roped), (k_parts, roped_k))[k]
                nc.scalar.copy(dst[:, 0], src[:, 2]).then_inc(part1_done.sem, 1)

            def copy_v(t, par):
                bank = misc_wait(act, "v0", t)
                if not (fixed(t) and t < 1):
                    wait(act, pv_unit, t - 1, len(UNITS))
                nc.scalar.copy(v_ones[:, 1 - par, :, :, 0:HD],
                               bank[:, 0:NB * 32].rearrange("p (n g d) -> p n g d", n=NB, d=HD)).then_inc(v_done.sem, 1)

            def minus1(t, i):
                bank = misc_wait(act, f"m{i}", t)
                if not (fixed(t) and t == -1):
                    wait(act, max_in[i], t, 32)
                nc.scalar.activation(minus_max[:, 0, i], bank[0:H, 0:P], ACT.Copy, scale=-1.0)\
                    .then_inc(minus1_done.sem, 1)

            def exponentiate(t, n):
                wait(act, scores_done, t, n + 1)
                u = n // KH
                if n % KH == 0 and not (fixed(t) and t == 0 and u < 2):
                    wait(act, pv_unit, t, u - 1)
                nc.scalar.activation(probs[:, u % 2, n % KH].rearrange("p h q -> p (h q)"), er[:, n % PV_RING],
                                     ACT.Exp, scale=EXP_SCALE).then_inc(exp_done.sem, 1)

            def copy_tile(t, n):
                bank = misc_wait(act, f"tx{n}", t)
                if not (fixed(t) and t == 0 and n == 0):
                    prev = made[f"th{n - 1}"] if n else made[f"th{PER_TURN - 1}"]
                    wait(act, prev, t if n else t - 1, 1)
                nc.scalar.copy(tileT[:], bank[:, 0:P]).then_inc(tileT_done.sem, 1)

            def tanh_tile(t, n):
                wait(act, pre_done, t, n + 1)
                if not (fixed(t) and t == 0 and n == 0):
                    wait(act, hid_done, t, n)
                nc.scalar.activation(pre_tanh[:], pre[:], ACT.Tanh, scale=0.5).then_inc(pre_tanh_done.sem, 1)

            def copy_o(t):
                bank = misc_wait(act, "oT0", t)
                nc.scalar.copy(oT[:], bank).then_inc(oT_done.sem, 1)

            def turn(t, par, main, prep, tiles):
                for step in range(STEPS):
                    if main:
                        exponentiate(t, step)
                    for kind, n in events(step):
                        if prep and kind == "a":
                            copy_a(t)
                        if prep and kind == "v":
                            copy_v(t, par)
                        if prep and kind == "m":
                            minus1(t, n)
                        if tiles and kind == "tx":
                            copy_tile(t, n)
                        if tiles and kind == "th":
                            tanh_tile(t, n)
                    if prep and step == 8:
                        part1(t, 0)
                        part1(t, 1)
                if prep:
                    minus1(t, NB - 1)
                if main:
                    copy_o(t)

            turn(-1, 1, False, True, False)
            act.wait_ge(route, ROUTE_SHIFTED)
            nc.scalar.activation(expd[:], shifted[:], ACT.Exp).then_inc(exp_route, 1)
            act.wait_ge(experts_in, 12 * 16)
            nc.scalar.activation(experts[:, :, 0:FE], experts[:, :, 0:FE], ACT.Copy, scale=rms_w[:, 0:1])\
                .then_inc(folded, 1)
            nc.scalar.mul(experts[:, :, FE:2 * FE], experts[:, :, FE:2 * FE], 0.5).then_inc(folded, 1)
            turn(0, 0, True, True, True)
            with act.Fori(0, (B - 2) // 2) as half:
                turn(half * 2 + 1, 1, True, True, True)
                turn(half * 2 + 2, 0, True, True, True)
            turn(B - 1, 1, True, False, False)

            def tanh_y(b, par):
                wait(act, y_scaled, b, 1)
                wait(act, y_silu_done, b - 1, 1) if not (fixed(b) and b == 0) else wait(act, hid_done, TURNS_OF_TILES, 0)
                nc.scalar.activation(pre_tanh[:], y[:, par], ACT.Tanh, scale=0.5).then_inc(y_tanh_done.sem, 1)

            tanh_y(0, 0)
            tanh_y(1, 1)
            with act.Fori(1, B // 2) as pair:
                tanh_y(pair * 2, 0)
                tanh_y(pair * 2 + 1, 1)

        @block.vector
        def _(dve):
            n_const = 0

            def const(ins):
                nonlocal n_const
                n_const += 1
                ins.then_inc(consts, 1)

            const(nc.vector.memset(minus_half[:], -0.5))
            const(nc.vector.memset(nobody[:], 0.0))
            dve.wait_ge(consts, 2)
            const(nc.vector.memset(nobody[:, D:].bitcast(I32), NOBODY))
            const(nc.vector.memset(ones[:], 1.0))
            const(nc.vector.memset(k_stack[:], 1.0))
            const(nc.vector.memset(v_ones[:], 0.0))
            dve.wait_ge(consts, 6)
            const(nc.vector.memset(v_ones[:, :, :, :, HD:HD + 1], 1.0))
            const(nc.vector.memset(running[:], 0.0))
            const(nc.vector.memset(ends[:], 0.0))
            assert n_const == N_CONSTS
            dve.wait_ge(w_in, 16 * N_W)
            q_of = wqb_in[:].rearrange("k (h p e) -> k e p h", p=HD // 2, e=2)
            kv_of = wkvb_in[QL:].rearrange("k (g p e v) -> k v e p g", p=HD // 2, e=2, v=2)
            for swap in range(2):
                for e in range(2):
                    q_to = wqb[:, swap].rearrange("k (p e h) -> k e p h", e=2, h=H)
                    nc.vector.tensor_copy(q_to[:, e], q_of[:, 1 - e if swap else e]).then_inc(wqb_done, 1)
            for v in range(3):
                if v < 2:
                    for e in range(2):
                        k_to = wkvb[QL:, v].rearrange("k (p e g) -> k e p g", e=2, g=KH)
                        ins = nc.vector.tensor_copy(k_to[:, e], kv_of[:, 0, 1 - e if v else e])
                        if v == 1 and e == 1:
                            ins.then_inc(wqb_done, 1)
                else:
                    nc.vector.tensor_copy(wkvb[QL:, 2], wkvb_in[QL:].rearrange("k (c v) -> k v c", v=2)[:, 1])\
                        .then_inc(wqb_done, 1)
            dve.wait_ge(turned, 1)
            nc.vector.tensor_scalar(gate_T[:], mr[:, 0, 0:E], rms_w[:, 0:1], None, ALU.mult).then_inc(gate_ready, 1)
            dve.wait_ge(turned, 2)
            nc.vector.tensor_copy(experts[:, :, 2 * FE:2 * FE + EC],
                                  mr[:, 1, 0:E * EC].rearrange("p (e c) -> p e c", c=EC)).then_inc(b1_ready, 1)

            steps = 0

            def step_of(ins, then=None):
                nonlocal steps
                steps += 1
                ins.then_inc(route, 1)
                dve.wait_ge(route, steps)
                if then:
                    assert steps == then, (steps, then)

            var, rstd = moments_all[:, :, :, 1], scale2_all[:]
            step_of(nc.vector.tensor_tensor(rms[:, 0].rearrange("p (b n) -> p b n", n=NB), var, rstd, ALU.mult))
            step_of(nc.vector.tensor_tensor(rms[:, 1].rearrange("p (b n) -> p b n", n=NB),
                                            rms[:, 0].rearrange("p (b n) -> p b n", n=NB), rstd, ALU.mult))
            step_of(nc.vector.tensor_scalar(rms[:, 2], rms[:, 1], RMS_EPS, None, ALU.add), ROUTE_MS)
            dve.wait_ge(rms_step, 1)
            dve.wait_ge(logits_made, 1)
            step_of(nc.vector.tensor_tensor(logits[:], er[:, 0, 0:B * NB * E].rearrange("p (n e) -> p n e", e=E),
                                            rms[:, 0, :, None].to_broadcast([P, B * NB, E]), ALU.mult))
            step_of(nc.vector.tensor_reduce(top[:], logits[:], AX.X, ALU.max))
            top_b = top[:, :, None].to_broadcast([P, B * NB, E])
            step_of(nc.vector.tensor_tensor(shifted[:], logits[:], top_b, ALU.subtract), ROUTE_SHIFTED)
            step_of(nc.vector.tensor_tensor(pick[:], logits[:], top_b, ALU.is_lt))
            dve.wait_ge(pool_consts, 6)
            numbers = number[:, None, 0:E].to_broadcast([P, B * NB, E])
            step_of(nc.vector.scalar_tensor_tensor(out=pick[:], in0=pick[:], scalar=float(E), in1=numbers,
                                                   op0=ALU.mult, op1=ALU.add))
            step_of(nc.vector.tensor_reduce(first[:], pick[:], AX.X, ALU.min))
            step_of(nc.vector.tensor_tensor(onehot[:], first[:, :, None].to_broadcast([P, B * NB, E]), numbers,
                                            ALU.is_equal), ROUTE_ONEHOT)

            def rope(t, k):
                for swap in range(2):
                    name = (("q0", "q_swap0"), ("k0", "k_swap0"))[k][swap]
                    dst, table = ((roped, rope_q), (roped_k, rope_k))[k]
                    bank = misc_wait(dve, name, t)[0:dst.shape[0]]
                    if not (fixed(t) and t == -1):
                        wait(dve, rope_add, t, k + 1)
                    nc.vector.tensor_tensor(dst[:, swap], bank, table[:, swap], ALU.mult).then_inc(rope_mult.sem, 1)

            def reduce_max(t, n):
                i, h0 = MAX_BANKS[n]
                heads, keys = HEADS_IN[i], P * (i + 1)
                wait(dve, max_made, t + 1, n + 1)
                if h0 == 0 and not (fixed(t) and t == -1):
                    wait(dve, made[f"m{i}"], t, 1)
                nc.vector.tensor_reduce(maxima[:, i, h0:h0 + heads],
                                        mr[:, n % 2, 0:heads * keys].rearrange("p (h k) -> p h k", h=heads),
                                        AX.X, ALU.max).then_inc(max_done.sem, 1)

            def minus2(t, i):
                wait(dve, minus1_done, t + 1, i + 1)
                if not (fixed(t) and t == -1):
                    wait(dve, max_in[i], t, 32)
                nc.vector.scalar_tensor_tensor(out=minus_max[:, 1, i], in0=bank_of(f"m{i}")[0:H, 0:P], scalar=-1.0,
                                               in1=minus_max[:, 0, i], op0=ALU.mult, op1=ALU.subtract)\
                    .then_inc(minus2_done.sem, 1)

            def copy_sums(t, i):
                wait(dve, pv_unit, t, UNITS.index((i, i)) + 1)
                if not (fixed(t) and t == 0 and i == 0):
                    wait(dve, made[f"o{i - 1 if i else NB - 1}"], t if i else t - 1, 1)
                nc.vector.tensor_copy(sums[:].rearrange("p h q -> p (h q)"), pv[:]).then_inc(sums_done.sem, 1)

            def divide(t, i):
                bank = misc_wait(dve, f"o{i}", t).rearrange("p (h g e) -> p h g e", h=KH, e=32)
                nc.vector.reciprocal(rden[:], bank[:, :, :, HD]).then_inc(rden_done.sem, 1)
                wait(dve, rden_done, t, i + 1)
                if i == 0 and not (fixed(t) and t == 0):
                    wait(dve, made["oT0"], t - 1, 1)
                nc.vector.tensor_tensor(o_rows[:, i].rearrange("p (g h d) -> p h g d", g=KH, h=KH), bank[:, :, :, 0:HD],
                                        rden[:, :, :, None].to_broadcast([P, KH, KH, HD]), ALU.mult)\
                    .then_inc(o_done.sem, 1)

            def keep_s(t):
                bank = misc_wait(dve, "s0", t).rearrange("p (n d) -> p n d", n=NB)
                nc.vector.tensor_tensor(xn2T_all[:, t].rearrange("p (n d) -> p n d", n=NB), bank,
                                        b_out[:, None, :].to_broadcast([P, NB, D]), ALU.add).then_inc(s_done.sem, 1)

            def tile_pre(t, n):
                bank = misc_wait(dve, f"th{n}", t).rearrange("p (c q) -> p c q", c=EC)
                if not (fixed(t) and t == 0 and n == 0):
                    wait(dve, hid_done, t, n)
                nc.vector.tensor_tensor(pre[:], bank, w_tile[:, n % 2, 2 * FE:2 * FE + EC, None].to_broadcast([P, EC, P]),
                                        ALU.add).then_inc(pre_done.sem, 1)

            def tile_hid(t, n):
                wait(dve, pre_tanh_done, t, n + 1)
                if not (fixed(t) and t == 0 and n == 0):
                    wait(dve, made[f"ty{n - 1 if n else PER_TURN - 1}"], t if n else t - 1, 1)
                nc.vector.scalar_tensor_tensor(out=hid[:], in0=pre_tanh[:], scalar=1.0, in1=pre[:], op0=ALU.add,
                                               op1=ALU.mult).then_inc(hid_done.sem, 1)

            def tile_add(t, n):
                bank = misc_wait(dve, f"ty{n}", t)
                if not (fixed(t) and t == 0 and n < 2):
                    wait(dve, tile_out_done[n % 2], t, 16 * (n // 2))
                nc.vector.tensor_tensor(tile_out[:, n % 2], bank[:, 0:D], w_tile[:, n % 2, 2 * FE + EC:], ALU.add)\
                    .then_inc(tile_done.sem, 1)

            def turn(t, par, main, prep, tiles):
                for step in range(STEPS):
                    if prep and step == 5:
                        rope(t, 0)
                    if prep and step == 6:
                        rope(t, 1)
                    if prep:
                        for n in max_banks(step):
                            reduce_max(t, n)
                    for kind, n in events(step):
                        if prep and kind == "m":
                            minus2(t, n)
                        if main and kind == "o":
                            divide(t, n)
                        if tiles and kind == "th":
                            tile_pre(t, n)
                            tile_hid(t, n)
                        if tiles and kind == "ty":
                            tile_add(t, n)
                    for i in range(NB - 1):
                        if main and step == 4 * UNITS.index((i, i)) + 7:
                            copy_sums(t, i)
                if prep:
                    minus2(t, NB - 1)
                if main:
                    copy_sums(t, NB - 1)
                    divide(t, NB - 1)
                    keep_s(t)

            dve.wait_ge(consts, N_CONSTS)
            turn(-1, 1, False, True, False)

            dve.wait_ge(counted, 1)
            dve.wait_ge(exp_route, 1)
            totals = er[:, 2, 0:B * NB * E].rearrange("p (n e) -> p n e", e=E)
            step_of(nc.vector.tensor_copy(running[:, 0, HALF:], totals))
            now, stride = 0, 1
            while stride <= HALF:
                step_of(nc.vector.tensor_tensor(running[:, 1 - now, HALF:], running[:, now, HALF:],
                                                running[:, now, HALF - stride:HALF - stride + B * NB], ALU.add))
                now, stride = 1 - now, 2 * stride
            step_of(nc.vector.tensor_scalar(tiles_i[:, 0], running[:, now, HALF + B * NB - 1], float(P - 1), None, ALU.add))
            step_of(nc.vector.tensor_scalar(tiles_i[:, 1], tiles_i[:, 0], 7, None, ALU.arith_shift_right))
            step_of(nc.vector.tensor_copy(ends[:, 0, 4:], tiles_i[:, 1]))
            e_now, stride = 0, 1
            step_of(nc.vector.tensor_copy(ends[:, 2, 4:], tiles_i[:, 1]))
            while stride < E:
                step_of(nc.vector.tensor_tensor(ends[:, 1 - e_now, 4:], ends[:, e_now, 4:],
                                                ends[:, e_now, 4 - stride:4 - stride + E], ALU.add))
                e_now, stride = 1 - e_now, 2 * stride
            end = ends[:, e_now, 4:]
            step_of(nc.vector.tensor_tensor(over[:], number[:, :, None].to_broadcast([P, TILES, E]),
                                            end[:, None, :].to_broadcast([P, TILES, E]), ALU.is_ge))
            step_of(nc.vector.tensor_reduce(tile_f[:], over[:], AX.X, ALU.add))
            step_of(nc.vector.tensor_scalar(tile_expert[:], tile_f[:], float(E - 1), None, ALU.min), ROUTE_EXPERTS)
            step_of(nc.vector.tensor_tensor(place_f[:], running[:, now, HALF:], totals, ALU.subtract))
            step_of(nc.vector.tensor_tensor(place_f[:], place_f[:],
                                            er[:, 1, 0:B * NB * E].rearrange("p (n e) -> p n e", e=E), ALU.add), ROUTE_PLACE)
            step_of(nc.vector.tensor_tensor(ends[:, 1 - e_now, 4:], end, ends[:, 2, 4:], ALU.subtract))
            starts = ends[:, 1 - e_now, None, 4:].to_broadcast([P, B * NB, E])
            step_of(nc.vector.scalar_tensor_tensor(out=place_f[:], in0=starts, scalar=float(P), in1=place_f[:],
                                                   op0=ALU.mult, op1=ALU.add))
            step_of(nc.vector.tensor_tensor(place_f[:], place_f[:], onehot[:], ALU.mult))
            step_of(nc.vector.tensor_reduce(pos_f[:], place_f[:], AX.X, ALU.add))
            step_of(nc.vector.tensor_copy(pos[:], pos_f[:]), ROUTE_POS)
            step_of(nc.vector.tensor_reduce(esum[:], expd[:], AX.X, ALU.add))
            step_of(nc.vector.reciprocal(score[:], esum[:]))
            step_of(nc.vector.tensor_tensor(rms[:, 1].rearrange("p (b n) -> p b n", n=NB),
                                            rms[:, 0].rearrange("p (b n) -> p b n", n=NB), rstd, ALU.mult))
            for n in range(B * NB):
                if n >= 4:
                    dve.wait_ge(sorted_in[n % 4], 16 * (n // 4))
                b, i = divmod(n, NB)
                nc.vector.tensor_scalar(to_sort[:, n % 4, 0:D], x_all[:, b, i], moments_all[:, b, i, 0:1],
                                        rms[:, 1, n:n + 1], ALU.subtract, ALU.mult).then_inc(to_sort_done, 1)
            turn(0, 0, True, True, True)
            with dve.Fori(0, (B - 2) // 2) as half:
                turn(half * 2 + 1, 1, True, True, True)
                turn(half * 2 + 2, 0, True, True, True)
            turn(B - 1, 1, True, False, False)

            def scale_y(b, pair, par):
                wait(dve, y_in[par], pair, 16)
                rows = score.rearrange("p (b n) -> p b n", n=NB)[:, b, :, None].to_broadcast([P, NB, D])
                nc.vector.tensor_tensor(y[:, par], y[:, par], rows, ALU.mult).then_inc(y_scaled.sem, 1)

            def combine(b, par):
                wait(dve, y_tanh_done, b, 1)
                if not (fixed(b) and b == 0):
                    wait(dve, result_done, b - 1, 1)
                nc.vector.scalar_tensor_tensor(out=hid[:], in0=pre_tanh[:], scalar=1.0, in1=y[:, par], op0=ALU.add,
                                               op1=ALU.mult).then_inc(y_silu_done.sem, 1)
                wait(dve, y_silu_done, b, 1)
                nc.vector.scalar_tensor_tensor(out=pre[:], in0=hid[:], scalar=0.5,
                                               in1=xn2T_all[:, b].rearrange("p (n d) -> p n d", n=NB),
                                               op0=ALU.mult, op1=ALU.mult).then_inc(gated_done.sem, 1)
                wait(dve, gated_done, b, 1)
                nc.vector.tensor_tensor(x_all[:, b], pre[:], x_all[:, b], ALU.add).then_inc(result_done.sem, 1)

            wait(dve, s_done, B, 0)
            scale_y(0, 0, 0)
            combine(0, 0)
            scale_y(1, 0, 1)
            combine(1, 1)
            with dve.Fori(1, B // 2) as pair:
                scale_y(pair * 2, pair, 0)
                combine(pair * 2, 0)
                scale_y(pair * 2 + 1, pair, 1)
                combine(pair * 2 + 1, 1)

        @block.gpsimd
        def _(pool):
            g = nc.gpsimd
            g.memset(before[:], 1.0).then_inc(pool_consts, 1)
            g.memset(mask[:], 0.0).then_inc(pool_consts, 1)
            g.tensor_copy(ident_b[:], ident[:]).then_inc(pool_consts, 1)
            pool.wait_ge(pool_consts, 2)
            g.affine_select(out=before[:], in_=before[:], compare_op=ALU.is_gt, fill=0.0, base=0, pattern=[[1, P]],
                            channel_multiplier=-1).then_inc(pool_consts, 1)
            g.affine_select(out=mask[:], in_=mask[:], compare_op=ALU.is_ge, fill=BIG, base=0, pattern=[[-1, P]],
                            channel_multiplier=1).then_inc(pool_consts, 1)
            g.iota(number[:], [[1, TILES]], base=0, channel_multiplier=0, allow_small_or_imprecise_dtypes=True)\
                .then_inc(pool_consts, 1)
            pool.wait_ge(route, ROUTE_MS)
            pool.wait_ge(consts, 1)
            g.tensor_tensor(rms[:, 0], rms[:, 2], minus_half[:], ALU.pow).then_inc(rms_step, 1)

            def prepare(t, k):
                dst, rest, parts = ((roped, q_rest, q_parts), (roped_k, k_rest, k_parts))[k]
                wait_apart(pool, rope_mult, t + 1, 2 * (k + 1), passed)
                if not (fixed(t) and t == -1):
                    wait_apart(pool, part1_done, t, k + 1, passed)
                g.tensor_tensor(dst[:, 2], dst[:, 0], dst[:, 1], ALU.add).then_inc(rope_add.sem, 1)
                wait_apart(pool, part1_done, t + 1, k + 1, passed)
                if not (fixed(t) and t == -1):
                    wait_apart(pool, part3_done, t, k + 1, passed)
                    wait_apart(pool, stack_in, t, STACK2_IN, passed)
                g.tensor_tensor(rest[:], dst[:, 2], parts[:, 0], ALU.subtract).then_inc(rest_done.sem, 1)
                wait_apart(pool, rest_done, t + 1, k + 1, passed)
                g.tensor_scalar(parts[:, 1], rest[:], 1.0, 1.0, ALU.mult, ALU.mult).then_inc(part2_done.sem, 1)
                wait_apart(pool, part2_done, t + 1, k + 1, passed)
                g.tensor_tensor(parts[:, 2], rest[:], parts[:, 1], ALU.subtract).then_inc(part3_done.sem, 1)

            def zero_behind(t, i, h):
                u = UNITS.index((i, i))
                wait_apart(pool, exp_done, t, KH * u + h + 1, passed)
                view = probs[:, u % 2, h]
                g.affine_select(out=view, in_=view, compare_op=ALU.is_ge, fill=0.0, base=0,
                                pattern=[[0, KH], [1, P]], channel_multiplier=-1).then_inc(masked.sem, 1)

            def send_tile(t, n):
                wait_apart(pool, tile_done, t, n + 1, passed)
                g.indirect_dma_start(expert_out, bass.IndirectOffsetOnAxis(ap=tile_in[:, n % 2, D:].bitcast(I32), axis=0),
                                     tile_out[:, n % 2], None, bounds_check=B * T - 1, oob_is_err=False)\
                    .then_inc(tile_out_done[n % 2].sem, 16)

            def turn(t, par, main, prep, tiles):
                for step in range(STEPS):
                    if prep and step == 7:
                        prepare(t, 0)
                        prepare(t, 1)
                    (i, j), h = UNITS[step // KH], step % KH
                    if main and i == j:
                        zero_behind(t, i, h)
                    for kind, n in events(step):
                        if tiles and kind == "ty":
                            send_tile(t, n)

            turn(-1, 1, False, True, False)
            for i in range(4):
                g.iota(to_sort[:, i, D:].bitcast(I32), [[0, 1]], base=P * i, channel_multiplier=1).then_inc(pool_consts, 1)
            pool.wait_ge(filled, 16)
            pool.wait_ge(route, ROUTE_POS)
            for n in range(B * NB):
                pool.wait_ge(to_sort_done, n + 1)
                pool.wait_ge(pool_consts, 10 + max(0, n - 3))
                g.indirect_dma_start(sorted_rows, bass.IndirectOffsetOnAxis(ap=pos[:, n:n + 1], axis=0),
                                     to_sort[:, n % 4], None).then_inc(sorted_in[n % 4], 16)
                if n + 4 < B * NB:
                    pool.wait_ge(sorted_in[n % 4], 16 * (n // 4 + 1))
                    g.iota(to_sort[:, n % 4, D:].bitcast(I32), [[0, 1]], base=P * (n + 4), channel_multiplier=1)\
                        .then_inc(pool_consts, 1)
            turn(0, 0, True, True, True)
            with pool.Fori(0, (B - 2) // 2) as half:
                turn(half * 2 + 1, 1, True, True, True)
                turn(half * 2 + 2, 0, True, True, True)
            turn(B - 1, 1, True, False, False)



ROUTE_MS, ROUTE_SHIFTED, ROUTE_ONEHOT = 3, 6, 10
ROUTE_EXPERTS, ROUTE_PLACE, ROUTE_POS = 26, 28, 33
N_CONSTS = 9


NAMES = ("L0_attn_hidden_states", "L0_attn_Wq", "L0_attn_Wk", "L0_attn_Wv", "L0_attn_Wo", "L0_ffn_w_gate",
         "L0_ffn_w_up", "L0_ffn_w_down", "L1_attn_Wqa", "L1_attn_Wqb", "L1_attn_Wkva", "L1_attn_Wkvb",
         "L1_attn_Wout", "L1_attn_bout", "L1_ffn_rms_w", "L1_ffn_gate_w", "L1_ffn_W1", "L1_ffn_b1", "L1_ffn_W2",
         "L1_ffn_b2")


def rope_tables():
    freq = (np.float32(1.0) / np.float32(ROPE_BASE) ** (np.arange(0, HD, 2, dtype=np.float32) / np.float32(HD)))
    angle = np.outer(freq.astype(np.float32), np.arange(T, dtype=np.float32)).astype(np.float32)
    cos, sin = np.cos(angle), np.sin(angle)
    both = np.stack([np.repeat(cos, 2, axis=0), np.stack([-sin, sin], axis=1).reshape(HD, T)], axis=1)
    return [np.ascontiguousarray(np.repeat(both, heads, axis=0).astype(np.float32)) for heads in (H, KH)]


def kernel(**inputs):
    import concourse.bacc as bacc
    from concourse.bass_utils import run_bass_kernel_spmd

    nc = bacc.Bacc("TRN2", target_bir_lowering=False, num_devices=1)
    arrays = {name: np.ascontiguousarray(inputs[name]) for name in NAMES}
    arrays["rope_q"], arrays["rope_k"] = rope_tables()
    aps = {name: nc.dram_tensor(name, a.shape, mybir.dt.from_np(a.dtype), kind="ExternalInput").ap()
           for name, a in arrays.items()}
    out = nc.dram_tensor("out", (B, T, D), F32, kind="ExternalOutput").ap()
    program(nc, aps, out)
    return run_bass_kernel_spmd(nc, [arrays], core_ids=[0]).results[0]["out"]
```
